# Optimizing a Trainium2 kernel written in Bass

```python
import numpy as np
import jax
import jax.numpy as jnp

def _softmax(x, axis=-1):
    return jax.nn.softmax(x, axis=axis)

def _gelu(x):
    return jax.nn.gelu(x, approximate=True)

def _silu(x):
    return jax.nn.silu(x)

def _sigmoid(x):
    return jax.nn.sigmoid(x)

def _layernorm(x, axis=-1, eps=1e-05):
    m = jnp.mean(x, axis=axis, keepdims=True)
    v = jnp.var(x, axis=axis, keepdims=True)
    return (x - m) / jnp.sqrt(v + eps)

def _scatter_add(tgt, idx, src, axis=0):
    return tgt.at[idx].add(src)

def _segment_sum(src, seg, n):
    return jax.ops.segment_sum(src, seg, n)
kernel_name = 'mk_adj_resnorm_d1_adj_r2_261cc5'

def setup_inputs(seed: int=0):
    np.random.seed(seed)
    _w = jnp.asarray

    def _rec_inputs():
        import jax
        import jax.numpy as jnp
        _gk = jax.random.key(seed)
        x = -8.776e-05 + 1 * jax.random.normal(jax.random.fold_in(_gk, 1), (4096, 256), jnp.float32)
        _a = jax.random.bernoulli(jax.random.fold_in(_gk, 2), 0.000976562, (4096, 4096))
        _a = jnp.logical_or(_a, jnp.eye(4096, dtype=bool))
        _af = _a.astype(jnp.float32)
        _af = _af * jax.random.uniform(jax.random.fold_in(_gk, 3), (4096, 4096), jnp.float32, 0.05, 1)
        adj = _af
        return (x, adj)
    x, adj = _rec_inputs()

    def _L0_gnn_setup():
        import jax, jax.numpy as jnp
        import numpy as np
        N = 5000
        IN_F = 256
        OUT_F = 256
        key = jax.random.key(seed)
        k1, k2, k3 = jax.random.split(key, 3)
        x = jax.random.normal(k1, (N, IN_F), dtype=jnp.float32)
        adj = jax.random.uniform(k2, (N, N), dtype=jnp.float32)
        stdv = 1.0 / np.sqrt(OUT_F)
        weight = jax.random.uniform(k3, (IN_F, OUT_F), dtype=jnp.float32, minval=-stdv, maxval=stdv)
        t = jnp.ones((1,), dtype=jnp.float32)
        return {'x': x, 'adj': adj, 't': t, 'weight': weight}
    _L0_gnn_all = _L0_gnn_setup()
    _L0_gnn_in = {k: v for k, v in _L0_gnn_all.items() if k in ('t', 'weight')}
    del _L0_gnn_all
    return {'x': x, 'adj': adj, 'L0_gnn_t': _L0_gnn_in['t'], 'L0_gnn_weight': _L0_gnn_in['weight']}

def reference(x, adj, L0_gnn_t, L0_gnn_weight):
    import jax
    import jax.numpy as jnp

    def _L0_gnn_ref(x, adj, t, weight):
        import jax, jax.numpy as jnp
        import numpy as np
        N = 5000
        IN_F = 256
        OUT_F = 256
        ts = t[0]
        support = x @ weight
        return (1.0 - ts) * support + ts * (adj @ support)
    x = _layernorm(x + _L0_gnn_ref(x, adj, L0_gnn_t, L0_gnn_weight), axis=-1)
    return x

_drawn_inputs = setup_inputs


def setup_inputs(seed=0):
    import zlib

    import numpy as np

    out = dict(_drawn_inputs(seed))
    spreads = {}
    factors = {}
    for name, (base, spread) in spreads.items():
        noise = np.random.default_rng([zlib.crc32(name.encode()), seed]).standard_normal(out[name].shape)
        drawn = base * np.exp(spread * noise) if base else spread * noise
        out[name] = jnp.asarray(drawn.astype(out[name].dtype))
    for name, factor in factors.items():
        out[name] = (out[name] * factor).astype(out[name].dtype)
    return out
```

```python
from contextlib import ExitStack

import concourse.bass as bass
import numpy as np
from concourse import mybir

P = 128
CHUNK_BLOCKS = 16
RING = 4
X_TILES = 4
EPS = 1e-5


def gnn_layernorm_kernel(nc, xT, x, adjT, t, W, out):
    f32, f32r = mybir.dt.float32, mybir.dt.float32r
    ALU, ACT = mybir.AluOpType, mybir.ActivationFunctionType

    nodes, feats = x.shape
    TILES = nodes // P
    KT = feats // P
    CHUNK = CHUNK_BLOCKS * P
    PER_TILE = TILES // CHUNK_BLOCKS
    PAIRS = TILES // 2
    X_CHUNKS = TILES // X_TILES
    GROUPS_PER_X = X_TILES // 2
    S_BANKS = 2 * GROUPS_PER_X
    S_ROUNDS = X_CHUNKS // 2
    assert PER_TILE == 2 and RING == 2 * PER_TILE and S_BANKS == 4

    ctx = ExitStack()
    with ctx:
        def sb(name, shape, dt=f32):
            return ctx.enter_context(nc.sbuf_tensor(name, shape, dt))

        def sem(name):
            return ctx.enter_context(nc.semaphore(name))

        def sems(name, n):
            return [sem(f"{name}{i}") for i in range(n)]

        w_raw = sb("w_raw", [P, KT, feats])
        w_hi = sb("w_hi", [P, KT, feats], f32r)
        w_lo = sb("w_lo", [P, KT, feats], f32r)
        x_raw = sb("x_raw", [P, 2, KT, X_TILES * P])
        x_hi = sb("x_hi", [P, 2, KT, X_TILES * P], f32r)
        x_lo = sb("x_lo", [P, 2, KT, X_TILES * P], f32r)
        S = sb("S", [P, TILES, 2 * feats], f32r)
        a_raw = sb("a_raw", [P, RING, CHUNK])
        a_hi = sb("a_hi", [P, RING, CHUNK], f32r)
        a_lo = sb("a_lo", [P, RING, CHUNK], f32r)
        t_col = sb("t_col", [P, 1])
        omt_col = sb("omt_col", [P, 1])
        eps_col = sb("eps_col", [P, 1])
        x_rows = sb("x_rows", [P, 2, feats])
        base = sb("base", [P, 2, feats])
        s_sum = sb("s_sum", [P, 2, feats])
        s_scaled = sb("s_scaled", [P, 2, feats])
        y_part = sb("y_part", [P, feats])
        y = sb("y", [P, feats])
        stats = sb("stats", [P, 6])
        mean_var = sb("mean_var", [P, 2])
        std = sb("std", [P, 1])
        rstd = sb("rstd", [P, 1])
        normed = sb("normed", [P, 2, feats])

        s_ps = [ctx.enter_context(nc.psum_tensor(f"s_ps{i}", [P, 2, feats], f32)) for i in range(S_BANKS)]
        agg = [ctx.enter_context(nc.psum_tensor(f"agg{i}", [P, 2 * feats], f32)) for i in range(2)]

        w_loaded, t_loaded = sem("w_loaded"), sem("t_loaded")
        w_hi_ready, w_lo_ready = sem("w_hi_ready"), sem("w_lo_ready")
        eps_ready, omt_ready = sem("eps_ready"), sem("omt_ready")
        x_loaded = sems("x_loaded", 2)
        x_hi_ready, x_lo_ready = sems("x_hi_ready", 2), sems("x_lo_ready", 2)
        s_acc_ready = sems("s_acc_ready", S_BANKS)
        s_hi_ready = sems("s_hi_ready", S_BANKS)
        s_lo_ready = sems("s_lo_ready", S_BANKS)
        a_loaded = sems("a_loaded", RING)
        a_hi_ready, a_lo_ready = sems("a_hi_ready", RING), sems("a_lo_ready", RING)
        a_used = sems("a_used", RING)
        rows_loaded = sem("rows_loaded")
        s_sum_ready, s_scaled_ready, base_ready = sem("s_sum_ready"), sem("s_scaled_ready"), sem("base_ready")
        y_part_ready = sem("y_part_ready")
        y_ready = sems("y_ready", 2)
        stats_ready, mean_var_ready = sem("stats_ready"), sem("mean_var_ready")
        std_ready, rstd_ready, normed_ready = sem("std_ready"), sem("rstd_ready"), sem("normed_ready")
        stored = sems("stored", 2)

        block = ctx.enter_context(nc.Block())

        @block.sync
        def _(sp):
            def load_x(chunk, slot):
                sp.dma_start(x_raw[:, slot], xT[bass.ds(chunk, 1)].rearrange("c p k n -> p (c k) n")
                             ).then_inc(x_loaded[slot], 16)

            def load_adj(chunk, slot):
                sp.dma_start(a_raw[:, slot], adjT[bass.ds(chunk, 1)].rearrange("c p n -> p (c n)")
                             ).then_inc(a_loaded[slot], 16)

            def load_rows(pair):
                sp.dma_start(x_rows[:, :, :], x[bass.ds(pair * (2 * P), 2 * P)].rearrange("(u p) f -> p u f", p=P)
                             ).then_inc(rows_loaded, 16)

            def store(pair, u):
                sp.wait_ge(normed_ready, pair * 2 + (u + 1))
                sp.dma_start(out[bass.ds(pair * (2 * P) + u * P, P)], normed[:, u]).then_inc(stored[u], 16)

            sp.dma_start(w_raw[:, :, :], W.rearrange("(k p) n -> p k n", p=P)).then_inc(w_loaded, 16)
            load_x(0, 0)
            load_x(1, 1)
            sp.dma_start(t_col[:, :], t.partition_broadcast(P)).then_inc(t_loaded, 16)
            for r in range(1, S_ROUNDS):
                for u in range(2):
                    sp.wait_ge(x_lo_ready[u], r)
                    load_x(2 * r + u, u)
                load_adj(r - 1, r - 1)
            load_adj(RING - 1, RING - 1)
            load_rows(0)

            def refill(pair):
                for slot in range(RING):
                    sp.wait_ge(a_lo_ready[slot], pair + 1)
                    load_adj(pair * RING + (RING + slot), slot)
                sp.wait_ge(base_ready, pair + 1)
                load_rows(pair + 1)

            refill(0)
            with sp.Fori(1, PAIRS - 1) as pair:
                refill(pair)
                store(pair - 1, 0)
                store(pair - 1, 1)
            for pair in (PAIRS - 2, PAIRS - 1):
                store(pair, 0)
                store(pair, 1)
            for u in range(2):
                sp.wait_ge(stored[u], 16 * PAIRS)

        @block.scalar
        def _(act):
            def x_high(rnd, u):
                act.wait_ge(x_loaded[u], 16 * (rnd + 1))
                nc.scalar.activation(x_hi[:, u], x_raw[:, u], ACT.Copy).then_inc(x_hi_ready[u], 1)

            def s_high(rnd, u):
                for g in range(GROUPS_PER_X):
                    bank = GROUPS_PER_X * u + g
                    act.wait_ge(s_acc_ready[bank], rnd + 1)
                    tile = rnd * (2 * X_TILES) + 2 * bank
                    nc.scalar.activation(S[:, bass.ds(tile, 2), 0:feats], s_ps[bank][:, :, :], ACT.Copy
                                         ).then_inc(s_hi_ready[bank], 1)

            def a_high(rnd, slot):
                act.wait_ge(a_loaded[slot], 16 * (rnd + 1))
                act.wait_ge(a_used[slot], rnd)
                nc.scalar.activation(a_hi[:, slot], a_raw[:, slot], ACT.Copy).then_inc(a_hi_ready[slot], 1)

            def root(tile):
                act.wait_ge(mean_var_ready, tile + 1)
                nc.scalar.activation(std[:, :], mean_var[:, 1:2], ACT.Sqrt, bias=eps_col[:, :]
                                     ).then_inc(std_ready, 1)

            act.wait_ge(w_loaded, 16)
            nc.scalar.activation(w_hi[:, :, :], w_raw[:, :, :], ACT.Copy).then_inc(w_hi_ready, 1)
            x_high(0, 0)
            x_high(0, 1)
            with act.Fori(0, S_ROUNDS - 1) as rnd:
                for u in range(2):
                    s_high(rnd, u)
                    x_high(rnd + 1, u)
            a_high(0, 0)
            s_high(S_ROUNDS - 1, 0)
            s_high(S_ROUNDS - 1, 1)
            for slot in range(1, RING):
                a_high(0, slot)
            act.wait_ge(eps_ready, 1)
            with act.Fori(0, PAIRS - 1) as pair:
                for u in range(2):
                    a_high(pair + 1, 2 * u)
                    a_high(pair + 1, 2 * u + 1)
                    root(pair * 2 + u)
            root(TILES - 2)
            root(TILES - 1)

        @block.gpsimd
        def _(pool):
            nc.gpsimd.memset(eps_col[:, :], EPS).then_inc(eps_ready, 1)
            with pool.Fori(0, S_ROUNDS) as rnd:
                for u in range(2):
                    pool.wait_ge(x_hi_ready[u], rnd + 1)
                    nc.gpsimd.tensor_tensor(x_lo[:, u], x_raw[:, u], x_hi[:, u].bitcast(f32), ALU.subtract
                                            ).then_inc(x_lo_ready[u], 1)
            for bank in range(S_BANKS):
                pool.wait_ge(s_lo_ready[bank], S_ROUNDS)
            with pool.Fori(0, PAIRS) as pair:
                s_pair = S[:, bass.ds(pair * 2, 2), :].bitcast(f32)
                nc.gpsimd.tensor_tensor(s_sum[:, :, :], s_pair[:, :, 0:feats], s_pair[:, :, feats:2 * feats],
                                        ALU.add).then_inc(s_sum_ready, 1)
                pool.wait_ge(omt_ready, 1)
                pool.wait_ge(s_sum_ready, pair + 1)
                nc.gpsimd.tensor_tensor(s_scaled[:, :, :], s_sum[:, :, :],
                                        omt_col[:, :].unsqueeze(2).broadcast_to([P, 2, feats]), ALU.mult).then_inc(s_scaled_ready, 1)
                pool.wait_ge(s_scaled_ready, pair + 1)
                pool.wait_ge(rows_loaded, 16 * (pair + 1))
                for u in range(2):
                    pool.wait_ge(y_ready[u], pair)
                nc.gpsimd.tensor_tensor(base[:, :, :], s_scaled[:, :, :], x_rows[:, :, :], ALU.add
                                        ).then_inc(base_ready, 1)

        @block.vector
        def _(dve):
            def s_low(rnd, u):
                for g in range(GROUPS_PER_X):
                    bank = GROUPS_PER_X * u + g
                    dve.wait_ge(s_hi_ready[bank], rnd + 1)
                    tile = rnd * (2 * X_TILES) + 2 * bank
                    nc.vector.tensor_tensor(S[:, bass.ds(tile, 2), feats:2 * feats], s_ps[bank][:, :, :],
                                            S[:, bass.ds(tile, 2), 0:feats].bitcast(f32), ALU.subtract
                                            ).then_inc(s_lo_ready[bank], 1)

            def a_low(rnd, slot):
                dve.wait_ge(a_hi_ready[slot], rnd + 1)
                nc.vector.tensor_tensor(a_lo[:, slot], a_raw[:, slot], a_hi[:, slot].bitcast(f32), ALU.subtract
                                        ).then_inc(a_lo_ready[slot], 1)

            def layernorm(pair, u):
                tile = pair * 2 + u
                dve.wait_ge(a_used[2 * u + 1], pair + 1)
                dve.wait_ge(base_ready, pair + 1)
                nc.vector.scalar_tensor_tensor(y_part[:, :], agg[u][:, 0:feats], t_col[:, :], base[:, u],
                                               ALU.mult, ALU.add).then_inc(y_part_ready, 1)
                dve.wait_ge(y_part_ready, tile + 1)
                nc.vector.scalar_tensor_tensor(y[:, :], agg[u][:, feats:2 * feats], t_col[:, :], y_part[:, :],
                                               ALU.mult, ALU.add).then_inc(y_ready[u], 1)
                dve.wait_ge(y_ready[u], pair + 1)
                nc.vector.bn_stats(stats[:, :], y[:, :]).then_inc(stats_ready, 1)
                dve.wait_ge(t_loaded, 16)
                dve.wait_ge(stats_ready, tile + 1)
                nc.vector.bn_aggr(mean_var[:, :], stats[:, :]).then_inc(mean_var_ready, 1)
                dve.wait_ge(std_ready, tile + 1)
                nc.vector.reciprocal(rstd[:, :], std[:, :]).then_inc(rstd_ready, 1)
                dve.wait_ge(rstd_ready, tile + 1)
                dve.wait_ge(stored[u], 16 * pair)
                nc.vector.tensor_scalar(normed[:, u], y[:, :], mean_var[:, 0:1], rstd[:, :],
                                        ALU.subtract, ALU.mult).then_inc(normed_ready, 1)

            dve.wait_ge(w_hi_ready, 1)
            nc.vector.tensor_tensor(w_lo[:, :, :], w_raw[:, :, :], w_hi[:, :, :].bitcast(f32), ALU.subtract
                                    ).then_inc(w_lo_ready, 1)
            dve.wait_ge(t_loaded, 16)
            nc.vector.tensor_scalar(omt_col[:, :], t_col[:, :], -1.0, 1.0, ALU.mult, ALU.add).then_inc(omt_ready, 1)
            with dve.Fori(0, S_ROUNDS - 1) as rnd:
                s_low(rnd, 0)
                s_low(rnd, 1)
            a_low(0, 0)
            s_low(S_ROUNDS - 1, 0)
            s_low(S_ROUNDS - 1, 1)
            for slot in range(1, RING):
                a_low(0, slot)
            with dve.Fori(0, PAIRS - 1) as pair:
                for u in range(2):
                    a_low(pair + 1, 2 * u)
                    a_low(pair + 1, 2 * u + 1)
                    layernorm(pair, u)
            layernorm(PAIRS - 1, 0)
            layernorm(PAIRS - 1, 1)

        @block.tensor
        def _(pe):
            pe.wait_ge(w_lo_ready, 1)
            with pe.Fori(0, S_ROUNDS) as rnd:
                for u in range(2):
                    pe.wait_ge(x_lo_ready[u], rnd + 1)
                    for g in range(GROUPS_PER_X):
                        bank = GROUPS_PER_X * u + g
                        pe.wait_ge(s_lo_ready[bank], rnd)
                        for h in range(2):
                            cols = slice((2 * g + h) * P, (2 * g + h + 1) * P)
                            steps = [(xp, wp, k) for xp, wp in ((x_lo, w_hi), (x_hi, w_lo), (x_hi, w_hi))
                                     for k in range(KT)]
                            for n, (xp, wp, k) in enumerate(steps):
                                last = nc.tensor.matmul(s_ps[bank][:, h], xp[:, u, k, cols], wp[:, k],
                                                        start=(n == 0), stop=(n == len(steps) - 1))
                        last.then_inc(s_acc_ready[bank], 1)
            for bank in range(S_BANKS):
                pe.wait_ge(s_lo_ready[bank], S_ROUNDS)
            with pe.Fori(0, PAIRS) as pair:
                for u in range(2):
                    pe.wait_ge(y_ready[u], pair)
                    for c in range(PER_TILE):
                        slot = PER_TILE * u + c
                        pe.wait_ge(a_lo_ready[slot], pair + 1)
                        for b in range(CHUNK_BLOCKS):
                            j = c * CHUNK_BLOCKS + b
                            cols = slice(b * P, (b + 1) * P)
                            def high():
                                return nc.tensor.matmul(agg[u][:, :], a_hi[:, slot, cols], S[:, j],
                                                        start=(j == 0), stop=(j == TILES - 1))

                            def low():
                                return nc.tensor.matmul(agg[u][:, feats:], a_lo[:, slot, cols], S[:, j, 0:feats],
                                                        start=False, stop=False)
                            if j == 0:
                                high()
                                last = low()
                            else:
                                low()
                                last = high()
                        last.then_inc(a_used[slot], 1)


def kernel(x, adj, L0_gnn_t, L0_gnn_weight):
    import concourse.bacc as bacc
    from concourse.bass_utils import run_bass_kernel_spmd

    nodes, feats = x.shape
    tiles = nodes // P
    xT = x.reshape(tiles // X_TILES, X_TILES * P, feats // P, P).transpose(0, 3, 2, 1)
    adjT = adj.reshape(tiles, P, tiles // CHUNK_BLOCKS, CHUNK_BLOCKS, P).transpose(0, 2, 4, 3, 1)
    adjT = adjT.reshape(tiles * tiles // CHUNK_BLOCKS, P, CHUNK_BLOCKS * P)
    arrays = {"in_xT": xT, "in_x": x, "in_adjT": adjT, "in_t": L0_gnn_t, "in_W": L0_gnn_weight}
    arrays = {name: np.ascontiguousarray(a) for name, a in arrays.items()}

    nc = bacc.Bacc("TRN2", target_bir_lowering=False, num_devices=1)
    args = [nc.dram_tensor(name, a.shape, mybir.dt.from_np(a.dtype), kind="ExternalInput").ap()
            for name, a in arrays.items()]
    out = nc.dram_tensor("out", (nodes, feats), mybir.dt.float32, kind="ExternalOutput").ap()
    gnn_layernorm_kernel(nc, *args, out)
    return run_bass_kernel_spmd(nc, [arrays], core_ids=[0]).results[0]["out"]
```

```python
from contextlib import ExitStack

import concourse.bass as bass
import numpy as np
from concourse import mybir

P = 128
CHUNK_BLOCKS = 16
RING = 4
X_TILES = 2
X_RING = 4
EPS = 1e-5


def at_start(n):
    return isinstance(n, int) and n == 0


def gnn_layernorm_kernel(nc, xT, x, adjT, t, W, out):
    f32, f32r = mybir.dt.float32, mybir.dt.float32r
    ALU, ACT = mybir.AluOpType, mybir.ActivationFunctionType

    nodes, feats = x.shape
    TILES = nodes // P
    KT = feats // P
    CHUNK = CHUNK_BLOCKS * P
    PER_TILE = TILES // CHUNK_BLOCKS
    PAIRS = TILES // 2
    X_CHUNKS = TILES // X_TILES
    S_ROUNDS = X_CHUNKS // X_RING
    assert PER_TILE == 2 and RING == 2 * PER_TILE and S_ROUNDS <= RING

    ctx = ExitStack()
    with ctx:
        def sb(name, shape, dt=f32):
            return ctx.enter_context(nc.sbuf_tensor(name, shape, dt))

        def sem(name):
            return ctx.enter_context(nc.semaphore(name))

        def sems(name, n):
            return [sem(f"{name}{i}") for i in range(n)]

        w_raw = sb("w_raw", [P, KT, feats])
        w_hi = sb("w_hi", [P, KT, feats], f32r)
        w_lo = sb("w_lo", [P, KT, feats], f32r)
        x_raw = sb("x_raw", [P, X_RING, KT, X_TILES * P])
        x_hi = sb("x_hi", [P, X_RING, KT, X_TILES * P], f32r)
        x_lo = sb("x_lo", [P, X_RING, KT, X_TILES * P], f32r)
        S = sb("S", [P, TILES, 2 * feats], f32r)
        a_raw = sb("a_raw", [P, RING, CHUNK])
        a_hi = sb("a_hi", [P, RING, CHUNK], f32r)
        a_lo = sb("a_lo", [P, RING, CHUNK], f32r)
        t_col = sb("t_col", [P, 1])
        omt_col = sb("omt_col", [P, 1])
        x_rows = sb("x_rows", [P, 2, feats])
        base = sb("base", [P, 2, feats])
        s_sum = sb("s_sum", [P, 2, feats])
        s_scaled = sb("s_scaled", [P, 2, feats])
        y_part = sb("y_part", [P, feats])
        y = sb("y", [P, feats])
        stats = sb("stats", [P, 6])
        mean_var = sb("mean_var", [P, 2])
        var_eps = sb("var_eps", [P, 1])
        std = sb("std", [P, 1])
        rstd0 = sb("rstd0", [P, 1])
        newton_q = sb("newton_q", [P, 1])
        newton_c = sb("newton_c", [P, 1])
        rstd = sb("rstd", [P, 1])
        normed = sb("normed", [P, 2, feats])

        s_ps = [ctx.enter_context(nc.psum_tensor(f"s_ps{i}", [P, X_TILES, feats], f32)) for i in range(X_RING)]
        agg = [ctx.enter_context(nc.psum_tensor(f"agg{i}", [P, 2 * feats], f32)) for i in range(2)]

        w_loaded, t_loaded = sem("w_loaded"), sem("t_loaded")
        w_hi_ready, w_lo_ready = sem("w_hi_ready"), sem("w_lo_ready")
        omt_ready = sem("omt_ready")
        x_loaded = sems("x_loaded", X_RING)
        x_hi_ready, x_lo_ready = sems("x_hi_ready", X_RING), sems("x_lo_ready", X_RING)
        s_acc_ready = sems("s_acc_ready", X_RING)
        s_hi_ready = sems("s_hi_ready", X_RING)
        s_lo_ready = sems("s_lo_ready", X_RING)
        a_loaded = sems("a_loaded", RING)
        a_hi_ready, a_lo_ready = sems("a_hi_ready", RING), sems("a_lo_ready", RING)
        a_used = sems("a_used", RING)
        rows_loaded = sem("rows_loaded")
        s_sum_ready, s_scaled_ready, base_ready = sem("s_sum_ready"), sem("s_scaled_ready"), sem("base_ready")
        y_part_ready = sem("y_part_ready")
        y_ready = sems("y_ready", 2)
        stats_ready, mean_var_ready = sem("stats_ready"), sem("mean_var_ready")
        var_eps_ready, std_ready, rstd0_ready = sem("var_eps_ready"), sem("std_ready"), sem("rstd0_ready")
        newton_q_ready, newton_c_ready = sem("newton_q_ready"), sem("newton_c_ready")
        rstd_ready, normed_ready = sem("rstd_ready"), sem("normed_ready")
        stored = sems("stored", 2)

        block = ctx.enter_context(nc.Block())

        @block.sync
        def _(sp):
            def load_x(chunk, slot):
                sp.dma_start(x_raw[:, slot], xT[bass.ds(chunk, 1)].rearrange("c p k n -> p (c k) n")
                             ).then_inc(x_loaded[slot], 16)

            def load_adj(chunk, slot):
                sp.dma_start(a_raw[:, slot], adjT[bass.ds(chunk, 1)].rearrange("c p n -> p (c n)")
                             ).then_inc(a_loaded[slot], 16)

            def load_rows(pair):
                sp.dma_start(x_rows[:, :, :], x[bass.ds(pair * (2 * P), 2 * P)].rearrange("(u p) f -> p u f", p=P)
                             ).then_inc(rows_loaded, 16)

            def store(pair, u):
                sp.wait_ge(normed_ready, pair * 2 + (u + 1))
                sp.dma_start(out[bass.ds(pair * (2 * P) + u * P, P)], normed[:, u]).then_inc(stored[u], 16)

            load_x(0, 0)
            sp.dma_start(w_raw[:, :, :], W.rearrange("(k p) n -> p k n", p=P)).then_inc(w_loaded, 16)
            for slot in range(1, X_RING):
                load_x(slot, slot)
            sp.dma_start(t_col[:, :], t.partition_broadcast(P)).then_inc(t_loaded, 16)
            for r in range(1, S_ROUNDS):
                for slot in range(X_RING):
                    sp.wait_ge(x_lo_ready[slot], r)
                    load_x(r * X_RING + slot, slot)
                load_adj(r - 1, r - 1)
            for slot in range(S_ROUNDS - 1, RING):
                load_adj(slot, slot)
            load_rows(0)

            def refill(pair):
                for slot in range(RING):
                    sp.wait_ge(a_lo_ready[slot], pair + 1)
                    load_adj(pair * RING + (RING + slot), slot)
                sp.wait_ge(base_ready, pair + 1)
                load_rows(pair + 1)

            refill(0)
            with sp.Fori(1, PAIRS - 1) as pair:
                refill(pair)
                store(pair - 1, 0)
                store(pair - 1, 1)
            for pair in (PAIRS - 2, PAIRS - 1):
                store(pair, 0)
                store(pair, 1)
            for u in range(2):
                sp.wait_ge(stored[u], 16 * PAIRS)

        @block.scalar
        def _(act):
            def x_high(rnd, slot):
                act.wait_ge(x_loaded[slot], 16 * (rnd + 1))
                nc.scalar.activation(x_hi[:, slot], x_raw[:, slot], ACT.Copy).then_inc(x_hi_ready[slot], 1)

            def s_high(rnd, slot):
                act.wait_ge(s_acc_ready[slot], rnd + 1)
                tile = (rnd * X_RING + slot) * X_TILES
                nc.scalar.activation(S[:, bass.ds(tile, X_TILES), 0:feats], s_ps[slot][:, :, :], ACT.Copy
                                     ).then_inc(s_hi_ready[slot], 1)

            def a_high(rnd, slot):
                act.wait_ge(a_loaded[slot], 16 * (rnd + 1))
                if not at_start(rnd):
                    act.wait_ge(a_used[slot], rnd)
                nc.scalar.activation(a_hi[:, slot], a_raw[:, slot], ACT.Copy).then_inc(a_hi_ready[slot], 1)

            def root(tile):
                act.wait_ge(var_eps_ready, tile + 1)
                nc.scalar.activation(std[:, :], var_eps[:, :], ACT.Sqrt).then_inc(std_ready, 1)

            x_high(0, 0)
            act.wait_ge(w_loaded, 16)
            nc.scalar.activation(w_hi[:, :, :], w_raw[:, :, :], ACT.Copy).then_inc(w_hi_ready, 1)
            for slot in range(1, X_RING):
                x_high(0, slot)
            with act.Fori(0, S_ROUNDS - 1) as rnd:
                for slot in range(X_RING):
                    s_high(rnd, slot)
                    x_high(rnd + 1, slot)
            a_high(0, 0)
            for slot in range(X_RING):
                s_high(S_ROUNDS - 1, slot)
            for slot in range(1, RING):
                a_high(0, slot)
            with act.Fori(0, PAIRS - 1) as pair:
                for u in range(2):
                    a_high(pair + 1, 2 * u)
                    a_high(pair + 1, 2 * u + 1)
                    root(pair * 2 + u)
            root(TILES - 2)
            root(TILES - 1)

        @block.gpsimd
        def _(pool):
            with pool.Fori(0, S_ROUNDS) as rnd:
                for slot in range(X_RING):
                    pool.wait_ge(x_hi_ready[slot], rnd + 1)
                    nc.gpsimd.tensor_tensor(x_lo[:, slot], x_raw[:, slot], x_hi[:, slot].bitcast(f32), ALU.subtract
                                            ).then_inc(x_lo_ready[slot], 1)

            def make_base(pair):
                s_pair = S[:, bass.ds(pair * 2, 2), :].bitcast(f32)
                nc.gpsimd.tensor_tensor(s_sum[:, :, :], s_pair[:, :, 0:feats], s_pair[:, :, feats:2 * feats],
                                        ALU.add).then_inc(s_sum_ready, 1)
                pool.wait_ge(s_sum_ready, pair + 1)
                nc.gpsimd.tensor_tensor(s_scaled[:, :, :], s_sum[:, :, :],
                                        omt_col[:, :].unsqueeze(2).broadcast_to([P, 2, feats]), ALU.mult
                                        ).then_inc(s_scaled_ready, 1)
                pool.wait_ge(s_scaled_ready, pair + 1)
                pool.wait_ge(rows_loaded, 16 * (pair + 1))
                if not at_start(pair):
                    for u in range(2):
                        pool.wait_ge(y_ready[u], pair)
                nc.gpsimd.tensor_tensor(base[:, :, :], s_scaled[:, :, :], x_rows[:, :, :], ALU.add
                                        ).then_inc(base_ready, 1)

            pool.wait_ge(omt_ready, 1)
            for slot in range(X_RING):
                pool.wait_ge(s_lo_ready[slot], S_ROUNDS)
            make_base(0)
            with pool.Fori(1, PAIRS) as pair:
                make_base(pair)

        @block.vector
        def _(dve):
            def s_low(rnd, slot):
                dve.wait_ge(s_hi_ready[slot], rnd + 1)
                tile = (rnd * X_RING + slot) * X_TILES
                nc.vector.tensor_tensor(S[:, bass.ds(tile, X_TILES), feats:2 * feats], s_ps[slot][:, :, :],
                                        S[:, bass.ds(tile, X_TILES), 0:feats].bitcast(f32), ALU.subtract
                                        ).then_inc(s_lo_ready[slot], 1)

            def a_low(rnd, slot):
                dve.wait_ge(a_hi_ready[slot], rnd + 1)
                nc.vector.tensor_tensor(a_lo[:, slot], a_raw[:, slot], a_hi[:, slot].bitcast(f32), ALU.subtract
                                        ).then_inc(a_lo_ready[slot], 1)

            def layernorm(pair, u):
                tile = pair * 2 + u
                dve.wait_ge(a_used[2 * u + 1], pair + 1)
                dve.wait_ge(base_ready, pair + 1)
                nc.vector.scalar_tensor_tensor(y_part[:, :], agg[u][:, 0:feats], t_col[:, :], base[:, u],
                                               ALU.mult, ALU.add).then_inc(y_part_ready, 1)
                dve.wait_ge(y_part_ready, tile + 1)
                nc.vector.scalar_tensor_tensor(y[:, :], agg[u][:, feats:2 * feats], t_col[:, :], y_part[:, :],
                                               ALU.mult, ALU.add).then_inc(y_ready[u], 1)
                dve.wait_ge(y_ready[u], pair + 1)
                nc.vector.bn_stats(stats[:, :], y[:, :]).then_inc(stats_ready, 1)
                dve.wait_ge(t_loaded, 16)
                dve.wait_ge(stats_ready, tile + 1)
                nc.vector.bn_aggr(mean_var[:, :], stats[:, :]).then_inc(mean_var_ready, 1)
                dve.wait_ge(mean_var_ready, tile + 1)
                nc.vector.tensor_scalar(var_eps[:, :], mean_var[:, 1:2], EPS, None, ALU.add).then_inc(var_eps_ready, 1)
                dve.wait_ge(std_ready, tile + 1)
                nc.vector.reciprocal(rstd0[:, :], std[:, :]).then_inc(rstd0_ready, 1)
                dve.wait_ge(rstd0_ready, tile + 1)
                nc.vector.tensor_scalar(newton_q[:, :], rstd0[:, :], var_eps[:, :], rstd0[:, :], ALU.mult, ALU.mult
                                        ).then_inc(newton_q_ready, 1)
                dve.wait_ge(newton_q_ready, tile + 1)
                nc.vector.tensor_scalar(newton_c[:, :], newton_q[:, :], -0.5, 1.5, ALU.mult, ALU.add
                                        ).then_inc(newton_c_ready, 1)
                dve.wait_ge(newton_c_ready, tile + 1)
                nc.vector.tensor_tensor(rstd[:, :], newton_c[:, :], rstd0[:, :], ALU.mult).then_inc(rstd_ready, 1)
                dve.wait_ge(rstd_ready, tile + 1)
                if not at_start(pair):
                    dve.wait_ge(stored[u], 16 * pair)
                nc.vector.tensor_scalar(normed[:, u], y[:, :], mean_var[:, 0:1], rstd[:, :],
                                        ALU.subtract, ALU.mult).then_inc(normed_ready, 1)

            dve.wait_ge(w_hi_ready, 1)
            nc.vector.tensor_tensor(w_lo[:, :, :], w_raw[:, :, :], w_hi[:, :, :].bitcast(f32), ALU.subtract
                                    ).then_inc(w_lo_ready, 1)
            dve.wait_ge(t_loaded, 16)
            nc.vector.tensor_scalar(omt_col[:, :], t_col[:, :], -1.0, 1.0, ALU.mult, ALU.add).then_inc(omt_ready, 1)
            with dve.Fori(0, S_ROUNDS - 1) as rnd:
                for slot in range(X_RING):
                    s_low(rnd, slot)
            a_low(0, 0)
            for slot in range(X_RING):
                s_low(S_ROUNDS - 1, slot)
            for slot in range(1, RING):
                a_low(0, slot)

            def pair_of_tiles(pair):
                for u in range(2):
                    a_low(pair + 1, 2 * u)
                    a_low(pair + 1, 2 * u + 1)
                    layernorm(pair, u)

            pair_of_tiles(0)
            with dve.Fori(1, PAIRS - 1) as pair:
                pair_of_tiles(pair)
            layernorm(PAIRS - 1, 0)
            layernorm(PAIRS - 1, 1)

        @block.tensor
        def _(pe):
            def s_round(rnd):
                for slot in range(X_RING):
                    pe.wait_ge(x_hi_ready[slot], rnd + 1)
                    if at_start(rnd):
                        if slot == 0:
                            pe.wait_ge(w_hi_ready, 1)
                    else:
                        pe.wait_ge(s_lo_ready[slot], rnd)
                    for h in range(X_TILES):
                        cols = slice(h * P, (h + 1) * P)
                        for k in range(KT):
                            nc.tensor.matmul(s_ps[slot][:, h], x_hi[:, slot, k, cols], w_hi[:, k],
                                             start=(k == 0), stop=False)
                        if at_start(rnd) and slot == 0 and h == 0:
                            pe.wait_ge(w_lo_ready, 1)
                        for k in range(KT):
                            nc.tensor.matmul(s_ps[slot][:, h], x_hi[:, slot, k, cols], w_lo[:, k],
                                             start=False, stop=False)
                        if h == 0:
                            pe.wait_ge(x_lo_ready[slot], rnd + 1)
                        for k in range(KT):
                            last = nc.tensor.matmul(s_ps[slot][:, h], x_lo[:, slot, k, cols], w_hi[:, k],
                                                    start=False, stop=(k == KT - 1))
                    last.then_inc(s_acc_ready[slot], 1)

            def adj_round(pair):
                for u in range(2):
                    if not at_start(pair):
                        pe.wait_ge(y_ready[u], pair)
                    for c in range(PER_TILE):
                        slot = PER_TILE * u + c
                        pe.wait_ge(a_lo_ready[slot], pair + 1)
                        for b in range(CHUNK_BLOCKS):
                            j = c * CHUNK_BLOCKS + b
                            cols = slice(b * P, (b + 1) * P)
                            if at_start(pair) and u == 0 and j % X_TILES == 0:
                                x_chunk = j // X_TILES
                                pe.wait_ge(s_lo_ready[x_chunk % X_RING], x_chunk // X_RING + 1)

                            def high():
                                return nc.tensor.matmul(agg[u][:, :], a_hi[:, slot, cols], S[:, j],
                                                        start=(j == 0), stop=(j == TILES - 1))

                            def low():
                                return nc.tensor.matmul(agg[u][:, feats:], a_lo[:, slot, cols], S[:, j, 0:feats],
                                                        start=False, stop=False)
                            if j == 0:
                                high()
                                last = low()
                            else:
                                low()
                                last = high()
                        last.then_inc(a_used[slot], 1)

            s_round(0)
            with pe.Fori(1, S_ROUNDS) as rnd:
                s_round(rnd)
            adj_round(0)
            with pe.Fori(1, PAIRS) as pair:
                adj_round(pair)


def kernel(x, adj, L0_gnn_t, L0_gnn_weight):
    import concourse.bacc as bacc
    from concourse.bass_utils import run_bass_kernel_spmd

    nodes, feats = x.shape
    tiles = nodes // P
    xT = x.reshape(tiles // X_TILES, X_TILES * P, feats // P, P).transpose(0, 3, 2, 1)
    adjT = adj.reshape(tiles, P, tiles // CHUNK_BLOCKS, CHUNK_BLOCKS, P).transpose(0, 2, 4, 3, 1)
    adjT = adjT.reshape(tiles * tiles // CHUNK_BLOCKS, P, CHUNK_BLOCKS * P)
    arrays = {"in_xT": xT, "in_x": x, "in_adjT": adjT, "in_t": L0_gnn_t, "in_W": L0_gnn_weight}
    arrays = {name: np.ascontiguousarray(a) for name, a in arrays.items()}

    nc = bacc.Bacc("TRN2", target_bir_lowering=False, num_devices=1)
    args = [nc.dram_tensor(name, a.shape, mybir.dt.from_np(a.dtype), kind="ExternalInput").ap()
            for name, a in arrays.items()]
    out = nc.dram_tensor("out", (nodes, feats), mybir.dt.float32, kind="ExternalOutput").ap()
    gnn_layernorm_kernel(nc, *args, out)
    return run_bass_kernel_spmd(nc, [arrays], core_ids=[0]).results[0]["out"]
```
